# Optimizing a Trainium2 kernel written in Bass

```python
import numpy as np
import jax
import jax.numpy as jnp

def _softmax(x, axis=-1):
    return jax.nn.softmax(x, axis=axis)

def _gelu(x):
    return jax.nn.gelu(x, approximate=True)

def _silu(x):
    return jax.nn.silu(x)

def _sigmoid(x):
    return jax.nn.sigmoid(x)

def _layernorm(x, axis=-1, eps=1e-05):
    m = jnp.mean(x, axis=axis, keepdims=True)
    v = jnp.var(x, axis=axis, keepdims=True)
    return (x - m) / jnp.sqrt(v + eps)

def _scatter_add(tgt, idx, src, axis=0):
    return tgt.at[idx].add(src)

def _segment_sum(src, seg, n):
    return jax.ops.segment_sum(src, seg, n)
kernel_name = 'mk_gnn_resnorm_d4_gnn_r32_69cb88'

def setup_inputs(seed: int=0):
    np.random.seed(seed)
    _w = jnp.asarray

    def _rec_inputs():
        import jax
        import jax.numpy as jnp
        _gk = jax.random.key(seed)
        x = -0.0003713 + 1 * jax.random.normal(jax.random.fold_in(_gk, 1), (3125, 128), jnp.float32)
        _s = jax.random.randint(jax.random.fold_in(_gk, 2), (50000,), 0, 3125, jnp.int32)
        _d = jax.random.randint(jax.random.fold_in(_gk, 3), (50000,), 0, 3125, jnp.int32)
        _loop = jnp.arange(3125, dtype=jnp.int32)
        src = jnp.concatenate([_s, _d, _loop])
        dst = jnp.concatenate([_d, _s, _loop])
        _o = jnp.argsort(dst, stable=True)
        src = src[_o]
        dst = dst[_o]
        edge_weight = jax.random.uniform(jax.random.fold_in(_gk, 13), (103125,), jnp.float32, 0.0, 1)
        return (x, src, dst, edge_weight)
    x, src, dst, edge_weight = _rec_inputs()

    def _L0_gnn_setup():
        import jax, jax.numpy as jnp
        import numpy as np
        N_NODES = 3125
        N_EDGES = 50000
        D_IN = 128
        D_OUT = 128
        key = jax.random.key(seed)
        k1, k2, k3, k4, k5, k6 = jax.random.split(key, 6)
        x = jax.random.normal(k1, (N_NODES, D_IN), dtype=jnp.float32)
        edge_row = jax.random.randint(k2, (N_EDGES,), 0, N_NODES, dtype=jnp.int32)
        edge_col = jax.random.randint(k3, (N_EDGES,), 0, N_NODES, dtype=jnp.int32)
        edge_val = jax.random.uniform(k4, (N_EDGES,), dtype=jnp.float32)
        stdv = 1.0 / np.sqrt(D_OUT)
        weight = jax.random.uniform(k5, (D_IN, D_OUT), jnp.float32, -stdv, stdv)
        b = jax.random.uniform(k6, (D_OUT,), jnp.float32, -stdv, stdv)
        return {'x': x, 'edge_row': edge_row, 'edge_col': edge_col, 'edge_val': edge_val, 'weight': weight, 'b': b}
    _L0_gnn_all = _L0_gnn_setup()
    _L0_gnn_in = {k: v for k, v in _L0_gnn_all.items() if k in ('weight', 'b')}
    del _L0_gnn_all

    def _L1_gnn_setup():
        import jax, jax.numpy as jnp
        import numpy as np
        N = 3125
        E = 50000
        D_IN = 128
        D_OUT = 128
        HEADS = 4
        C = D_OUT // HEADS
        NEG_SLOPE = 0.2
        EPS_SOFTMAX = 1e-16
        EPS_LN = 1e-05

        def _gat_edge_conv(x, src, dst, W, att_src, att_dst, gat_bias, skip_W, skip_b, ln_g, ln_b):
            n = x.shape[0]
            h = (x @ W).reshape(n, HEADS, C)
            a_s = jnp.einsum('nhc,hc->nh', h, att_src)
            a_d = jnp.einsum('nhc,hc->nh', h, att_dst)
            e = jax.nn.leaky_relu(a_s[src] + a_d[dst], NEG_SLOPE)
            m = jax.ops.segment_max(e, dst, num_segments=n)
            p = jnp.exp(e - m[dst])
            z = jax.ops.segment_sum(p, dst, num_segments=n)
            alpha = p / (z[dst] + EPS_SOFTMAX)
            msg = h[src] * alpha[:, :, None]
            out = jax.ops.segment_sum(msg, dst, num_segments=n)
            out = out.reshape(n, HEADS * C) + gat_bias
            out = out + x @ skip_W + skip_b
            mu = out.mean(-1, keepdims=True)
            var = ((out - mu) ** 2).mean(-1, keepdims=True)
            return (out - mu) * jax.lax.rsqrt(var + EPS_LN) * ln_g + ln_b
        key = jax.random.key(seed)
        ks = jax.random.split(key, 10)
        x = jax.random.normal(ks[0], (N, D_IN), dtype=jnp.float32)
        edge_index = jax.random.randint(ks[1], (2, E), 0, N, dtype=jnp.int64)
        s = 1.0 / np.sqrt(D_IN)
        W = jax.random.normal(ks[2], (D_IN, HEADS * C), dtype=jnp.float32) * s
        att_src = jax.random.normal(ks[3], (HEADS, C), dtype=jnp.float32) * (1.0 / np.sqrt(C))
        att_dst = jax.random.normal(ks[4], (HEADS, C), dtype=jnp.float32) * (1.0 / np.sqrt(C))
        gat_bias = jax.random.normal(ks[5], (D_OUT,), dtype=jnp.float32) * 0.02
        skip_W = jax.random.normal(ks[6], (D_IN, D_OUT), dtype=jnp.float32) * s
        skip_b = jax.random.normal(ks[7], (D_OUT,), dtype=jnp.float32) * 0.02
        ln_g = jnp.ones((D_OUT,), dtype=jnp.float32)
        ln_b = jnp.zeros((D_OUT,), dtype=jnp.float32)
        return {'x': x, 'edge_index': edge_index, 'W': W, 'att_src': att_src, 'att_dst': att_dst, 'gat_bias': gat_bias, 'skip_W': skip_W, 'skip_b': skip_b, 'ln_g': ln_g, 'ln_b': ln_b}
    _L1_gnn_all = _L1_gnn_setup()
    _L1_gnn_in = {k: v for k, v in _L1_gnn_all.items() if k in ('W', 'att_src', 'att_dst', 'gat_bias', 'skip_W', 'skip_b', 'ln_g', 'ln_b')}
    del _L1_gnn_all

    def _L2_gnn_setup():
        import jax, jax.numpy as jnp
        import numpy as np
        N, D, E = (1250, 128, 20000)
        key = jax.random.key(seed)
        ks = jax.random.split(key, 6)
        x = jax.random.normal(ks[0], (N, D), dtype=jnp.float32)
        edge_index = jax.random.randint(ks[1], (2, E), 0, N, dtype=jnp.int64)
        s = 1.0 / np.sqrt(D)
        Wq = jax.random.normal(ks[2], (D, D), dtype=jnp.float32) * s
        Wk = jax.random.normal(ks[3], (D, D), dtype=jnp.float32) * s
        Wv = jax.random.normal(ks[4], (D, D), dtype=jnp.float32) * s
        Wo = jax.random.normal(ks[5], (D, D), dtype=jnp.float32) * s
        return {'x': x, 'Wq': Wq, 'Wk': Wk, 'Wv': Wv, 'Wo': Wo, 'edge_index': edge_index}
    _L2_gnn_all = _L2_gnn_setup()
    _L2_gnn_in = {k: v for k, v in _L2_gnn_all.items() if k in ('Wq', 'Wk', 'Wv', 'Wo')}
    del _L2_gnn_all

    def _L3_gnn_setup():
        import jax, jax.numpy as jnp
        import numpy as np
        N_NODES = 3125

        def _mean_aggregate(x, src, dst):
            msg_sum = jax.ops.segment_sum(x[src], dst, num_segments=N_NODES)
            deg = jax.ops.segment_sum(jnp.ones((src.shape[0],), x.dtype), dst, num_segments=N_NODES)
            return msg_sum / jnp.maximum(deg, 1.0)[:, None]

        def _sage_conv(x, src, dst, w_l, b_l, w_r):
            agg = _mean_aggregate(x, src, dst)
            return agg @ w_l + b_l + x @ w_r
        key = jax.random.key(seed)
        ks = jax.random.split(key, 8)
        in_dim, hid, out_dim = (128, 256, 128)
        E = 50000
        features = jax.random.normal(ks[0], (N_NODES, in_dim), dtype=jnp.float32)
        edge_index = jax.random.randint(ks[1], (2, E), 0, N_NODES, dtype=jnp.int64)
        s1 = 1.0 / np.sqrt(in_dim)
        s2 = 1.0 / np.sqrt(hid)
        return {'features': features, 'edge_index': edge_index, 'w1_l': jax.random.uniform(ks[2], (in_dim, hid), jnp.float32, -s1, s1), 'w1_r': jax.random.uniform(ks[3], (in_dim, hid), jnp.float32, -s1, s1), 'b1': jax.random.uniform(ks[4], (hid,), jnp.float32, -s1, s1), 'w2_l': jax.random.uniform(ks[5], (hid, out_dim), jnp.float32, -s2, s2), 'w2_r': jax.random.uniform(ks[6], (hid, out_dim), jnp.float32, -s2, s2), 'b2': jax.random.uniform(ks[7], (out_dim,), jnp.float32, -s2, s2)}
    _L3_gnn_all = _L3_gnn_setup()
    _L3_gnn_in = {k: v for k, v in _L3_gnn_all.items() if k in ('w1_l', 'w1_r', 'b1', 'w2_l', 'w2_r', 'b2')}
    del _L3_gnn_all
    return {'x': x, 'src': src, 'dst': dst, 'edge_weight': edge_weight, 'L0_gnn_weight': _L0_gnn_in['weight'], 'L0_gnn_b': _L0_gnn_in['b'], 'L1_gnn_W': _L1_gnn_in['W'], 'L1_gnn_att_src': _L1_gnn_in['att_src'], 'L1_gnn_att_dst': _L1_gnn_in['att_dst'], 'L1_gnn_gat_bias': _L1_gnn_in['gat_bias'], 'L1_gnn_skip_W': _L1_gnn_in['skip_W'], 'L1_gnn_skip_b': _L1_gnn_in['skip_b'], 'L1_gnn_ln_g': _L1_gnn_in['ln_g'], 'L1_gnn_ln_b': _L1_gnn_in['ln_b'], 'L2_gnn_Wq': _L2_gnn_in['Wq'], 'L2_gnn_Wk': _L2_gnn_in['Wk'], 'L2_gnn_Wv': _L2_gnn_in['Wv'], 'L2_gnn_Wo': _L2_gnn_in['Wo'], 'L3_gnn_w1_l': _L3_gnn_in['w1_l'], 'L3_gnn_w1_r': _L3_gnn_in['w1_r'], 'L3_gnn_b1': _L3_gnn_in['b1'], 'L3_gnn_w2_l': _L3_gnn_in['w2_l'], 'L3_gnn_w2_r': _L3_gnn_in['w2_r'], 'L3_gnn_b2': _L3_gnn_in['b2']}

def reference(x, src, dst, edge_weight, L0_gnn_weight, L0_gnn_b, L1_gnn_W, L1_gnn_att_src, L1_gnn_att_dst, L1_gnn_gat_bias, L1_gnn_skip_W, L1_gnn_skip_b, L1_gnn_ln_g, L1_gnn_ln_b, L2_gnn_Wq, L2_gnn_Wk, L2_gnn_Wv, L2_gnn_Wo, L3_gnn_w1_l, L3_gnn_w1_r, L3_gnn_b1, L3_gnn_w2_l, L3_gnn_w2_r, L3_gnn_b2):
    import jax
    import jax.numpy as jnp

    def _L0_gnn_ref(x, edge_row, edge_col, edge_val, weight, b):
        import jax, jax.numpy as jnp
        import numpy as np
        N_NODES = 3125
        N_EDGES = 50000
        D_IN = 128
        D_OUT = 128
        xw = x @ weight
        msgs = edge_val[:, None] * xw[edge_col]
        out = jax.ops.segment_sum(msgs, edge_row, num_segments=N_NODES)
        out = jax.nn.relu(out + b)
        return out

    def _L1_gnn_ref(x, edge_index, W, att_src, att_dst, gat_bias, skip_W, skip_b, ln_g, ln_b):
        import jax, jax.numpy as jnp
        import numpy as np
        N = 3125
        E = 50000
        D_IN = 128
        D_OUT = 128
        HEADS = 4
        C = D_OUT // HEADS
        NEG_SLOPE = 0.2
        EPS_SOFTMAX = 1e-16
        EPS_LN = 1e-05

        def _gat_edge_conv(x, src, dst, W, att_src, att_dst, gat_bias, skip_W, skip_b, ln_g, ln_b):
            n = x.shape[0]
            h = (x @ W).reshape(n, HEADS, C)
            a_s = jnp.einsum('nhc,hc->nh', h, att_src)
            a_d = jnp.einsum('nhc,hc->nh', h, att_dst)
            e = jax.nn.leaky_relu(a_s[src] + a_d[dst], NEG_SLOPE)
            m = jax.ops.segment_max(e, dst, num_segments=n)
            p = jnp.exp(e - m[dst])
            z = jax.ops.segment_sum(p, dst, num_segments=n)
            alpha = p / (z[dst] + EPS_SOFTMAX)
            msg = h[src] * alpha[:, :, None]
            out = jax.ops.segment_sum(msg, dst, num_segments=n)
            out = out.reshape(n, HEADS * C) + gat_bias
            out = out + x @ skip_W + skip_b
            mu = out.mean(-1, keepdims=True)
            var = ((out - mu) ** 2).mean(-1, keepdims=True)
            return (out - mu) * jax.lax.rsqrt(var + EPS_LN) * ln_g + ln_b
        n = x.shape[0]
        loops = jnp.arange(n, dtype=edge_index.dtype)
        src = jnp.concatenate([edge_index[0], loops])
        dst = jnp.concatenate([edge_index[1], loops])
        return _gat_edge_conv(x, src, dst, W, att_src, att_dst, gat_bias, skip_W, skip_b, ln_g, ln_b)

    def _L2_gnn_ref(x, Wq, Wk, Wv, Wo, edge_index):
        import jax, jax.numpy as jnp
        import numpy as np
        N, D, E = (1250, 128, 20000)
        num_nodes, d = x.shape
        scale = d ** (-0.5)
        sender, receiver = (edge_index[0], edge_index[1])
        Q = x @ Wq
        K = x @ Wk
        V = x @ Wv
        e = jnp.sum(Q[receiver] * K[sender], axis=-1) * scale
        m = jax.ops.segment_max(e, receiver, num_segments=num_nodes)
        m = jnp.where(jnp.isfinite(m), m, 0.0)
        w = jnp.exp(e - m[receiver])
        denom = jax.ops.segment_sum(w, receiver, num_segments=num_nodes)
        numer = jax.ops.segment_sum(w[:, None] * V[sender], receiver, num_segments=num_nodes)
        attn = jnp.where(denom[:, None] > 0, numer / jnp.maximum(denom, 1e-30)[:, None], 0.0)
        return x + attn @ Wo

    def _L3_gnn_ref(features, edge_index, w1_l, w1_r, b1, w2_l, w2_r, b2):
        import jax, jax.numpy as jnp
        import numpy as np
        N_NODES = 3125

        def _mean_aggregate(x, src, dst):
            msg_sum = jax.ops.segment_sum(x[src], dst, num_segments=N_NODES)
            deg = jax.ops.segment_sum(jnp.ones((src.shape[0],), x.dtype), dst, num_segments=N_NODES)
            return msg_sum / jnp.maximum(deg, 1.0)[:, None]

        def _sage_conv(x, src, dst, w_l, b_l, w_r):
            agg = _mean_aggregate(x, src, dst)
            return agg @ w_l + b_l + x @ w_r
        src, dst = (edge_index[0], edge_index[1])
        x = _sage_conv(features, src, dst, w1_l, b1, w1_r)
        x = jax.nn.relu(x)
        x = _sage_conv(x, src, dst, w2_l, b2, w2_r)
        return jax.nn.sigmoid(x)
    edge_index = jnp.stack([src, dst])
    x = _layernorm(x + _L0_gnn_ref(x, src, dst, edge_weight, L0_gnn_weight, L0_gnn_b), axis=-1)
    x = _layernorm(x + _L1_gnn_ref(x, edge_index, L1_gnn_W, L1_gnn_att_src, L1_gnn_att_dst, L1_gnn_gat_bias, L1_gnn_skip_W, L1_gnn_skip_b, L1_gnn_ln_g, L1_gnn_ln_b), axis=-1)
    x = _layernorm(x + _L2_gnn_ref(x, L2_gnn_Wq, L2_gnn_Wk, L2_gnn_Wv, L2_gnn_Wo, edge_index), axis=-1)
    x = _layernorm(x + _L3_gnn_ref(x, edge_index, L3_gnn_w1_l, L3_gnn_w1_r, L3_gnn_b1, L3_gnn_w2_l, L3_gnn_w2_r, L3_gnn_b2), axis=-1)
    return x

_drawn_inputs = setup_inputs


def setup_inputs(seed=0):
    import zlib

    import numpy as np

    out = dict(_drawn_inputs(seed))
    spreads = {'L1_gnn_ln_g': (1.0, 0.2), 'L1_gnn_ln_b': (0.0, 0.1)}
    factors = {'L1_gnn_gat_bias': 3.071,
     'L1_gnn_skip_b': 3.324,
     'L3_gnn_w1_l': 3.521,
     'L3_gnn_b1': 8.0,
     'L3_gnn_b2': 6.143}
    for name, (base, spread) in spreads.items():
        noise = np.random.default_rng([zlib.crc32(name.encode()), seed]).standard_normal(out[name].shape)
        drawn = base * np.exp(spread * noise) if base else spread * noise
        out[name] = jnp.asarray(drawn.astype(out[name].dtype))
    for name, factor in factors.items():
        out[name] = (out[name] * factor).astype(out[name].dtype)
    return out
```

```python
from contextlib import ExitStack

import concourse.bass as bass
from concourse import mybir

F32 = mybir.dt.float32
BF16 = mybir.dt.bfloat16
I32 = mybir.dt.int32
I16 = mybir.dt.int16
ALU = mybir.AluOpType
ACT = mybir.ActivationFunctionType
AX_X = mybir.AxisListType.X

P = 128
N = 3125
D = 128
E = 103125
NT = -(-N // P)
NP = NT * P
REST = N - (NT - 1) * P
BANK = 512
CW = 400
NCW = NP // CW
HALF = NP // 2
HB = NCW // 2
UN = 5
HEADS = 4
C = D // HEADS

NCH = -(-E // P)
ECT = -(-NCH // P)
ECOL = ECT * P
FULL = E // P
LASTN = E - FULL * P
WD = 16
NW = NP // WD
SL = CW
NSH = NP // SL
HW_ = NW // 2
BIG = 1.0e30
EPS_LN = 1e-5


class Kernel:

    def __init__(self, ins, out):
        self.out = out
        self.x = ins["x"]
        self.src = ins["src"]
        self.dst = ins["dst"]
        self.edge_weight = ins["edge_weight"]
        self.L0_gnn_weight = ins["L0_gnn_weight"]
        self.L0_gnn_b = ins["L0_gnn_b"]
        self.L1_gnn_W = ins["L1_gnn_W"]
        self.L1_gnn_att_src = ins["L1_gnn_att_src"]
        self.L1_gnn_att_dst = ins["L1_gnn_att_dst"]
        self.L1_gnn_gat_bias = ins["L1_gnn_gat_bias"]
        self.L1_gnn_skip_W = ins["L1_gnn_skip_W"]
        self.L1_gnn_skip_b = ins["L1_gnn_skip_b"]
        self.L1_gnn_ln_g = ins["L1_gnn_ln_g"]
        self.L1_gnn_ln_b = ins["L1_gnn_ln_b"]
        self.L2_gnn_Wq = ins["L2_gnn_Wq"]
        self.L2_gnn_Wk = ins["L2_gnn_Wk"]
        self.L2_gnn_Wv = ins["L2_gnn_Wv"]
        self.L2_gnn_Wo = ins["L2_gnn_Wo"]
        self.L3_gnn_w1_l = ins["L3_gnn_w1_l"]
        self.L3_gnn_w1_r = ins["L3_gnn_w1_r"]
        self.L3_gnn_b1 = ins["L3_gnn_b1"]
        self.L3_gnn_w2_l = ins["L3_gnn_w2_l"]
        self.L3_gnn_w2_r = ins["L3_gnn_w2_r"]
        self.L3_gnn_b2 = ins["L3_gnn_b2"]


class NormBuffers:
    def __init__(self, sb, layer):
        self.s6 = sb(f"{layer}_ln_s6", [P, NT, 6])
        self.mean = sb(f"{layer}_ln_mean", [P, NT])
        self.dif = sb(f"{layer}_ln_dif", [P, NT])
        self.var = sb(f"{layer}_ln_var", [P, NT])
        self.root = sb(f"{layer}_ln_root", [P, NT])


def edge_tables(nc, k):
    with ExitStack() as ctx:
        def sb(name, shape, dt=F32):
            return ctx.enter_context(nc.sbuf_tensor(name, shape, dt))

        src_i = sb("src_i", [P, ECT, P], I32)
        dst_i = sb("dst_i", [P, ECT, P], I32)
        ew = sb("ew", [P, ECT, P])
        dst = sb("dst_f", [P, ECT, P])
        src = sb("src_f", [P, ECT, P])
        hi = sb("src_hi", [P, ECT, P])
        rows = sb("edge_rows", [P, 5, ECT, P])
        part_b = sb("part_b", [P, ECT, P], BF16)
        left = sb("left", [P, ECT, P])
        tmp = sb("tmp", [P, ECT, P])
        cmax = sb("cmax", [P, ECT])
        cmin = sb("cmin", [P, ECT])
        cidx_i = sb("cidx_i", [P, ECT], I32)
        cidx = sb("cidx", [P, ECT])
        crev = sb("crev", [P, ECT])
        win_i = sb("win_i", [P, NW], I32)
        win = sb("win", [P, NW])
        pick = sb("pick", [P, NW])
        rng = sb("rng", [P, 2, NW])
        ends = sb("ends", [HW_, 4])
        first = sb("first", [HW_, 2])
        span = sb("span", [HW_, 2])
        pairs_i = sb("pairs_i", [HW_, 2], I32)
        pairs = sb("pairs", [HW_, 2])
        tri = sb("tri", [HW_, HW_])
        ones = sb("ones", [HW_, HW_])
        colf = sb("colf", [HW_, 2, 3])
        coli = sb("coli", [HW_, 2, 3], I32)
        base_i = sb("base_i", [P, NW], I32)
        ps = ctx.enter_context(nc.psum_tensor("ps_tab", [P, 8, BANK], F32))
        loaded = ctx.enter_context(nc.semaphore("loaded"))
        pool_done = ctx.enter_context(nc.semaphore("pool_done"))
        dve_done = ctx.enter_context(nc.semaphore("dve_done"))
        rows_ready = ctx.enter_context(nc.semaphore("rows_ready"))
        turned = ctx.enter_context(nc.semaphore("turned"))
        taken = ctx.enter_context(nc.semaphore("taken"))
        rng_ready = ctx.enter_context(nc.semaphore("rng_ready"))
        rng_turned = ctx.enter_context(nc.semaphore("rng_turned"))
        pairs_ready = ctx.enter_context(nc.semaphore("pairs_ready"))
        summed = ctx.enter_context(nc.semaphore("summed"))
        cols_ready = ctx.enter_context(nc.semaphore("cols_ready"))
        table_out = ctx.enter_context(nc.semaphore("table_out"))
        table_in = ctx.enter_context(nc.semaphore("table_in"))
        x_in = ctx.enter_context(nc.semaphore("x_in"))
        block = ctx.enter_context(nc.Block())
        PAD_SETS = 4

        @block.sync
        def _(sp):
            sp.wait_ge(pool_done, PAD_SETS)
            for dram, t in ((k.dst, dst_i), (k.src, src_i), (k.edge_weight, ew)):
                whole = (ECT - 1) * P
                sp.dma_start(t[:, 0:ECT - 1, :], dram[0:whole * P].rearrange("(t p e) -> p t e", p=P, e=P)
                             ).then_inc(loaded, 16)
                sp.dma_start(t[0:FULL - whole, ECT - 1, :],
                             dram[whole * P:FULL * P].rearrange("(p e) -> p e", e=P)).then_inc(loaded, 16)
                sp.dma_start(t[FULL - whole:FULL - whole + 1, ECT - 1, 0:LASTN],
                             dram[FULL * P:E].rearrange("(a e) -> a e", a=1)).then_inc(loaded, 16)
            sp.dma_start(k.X[:, 0:NT - 1, :], k.x[0:(NT - 1) * P, :].rearrange("(t p) d -> p t d", p=P)
                         ).then_inc(x_in, 16)
            sp.dma_start(k.X[0:REST, NT - 1, :], k.x[(NT - 1) * P:N, :]).then_inc(x_in, 16)
            sp.wait_ge(cols_ready, 1)
            sp.dma_start(k.table_d.rearrange("(h p) f -> p h f", h=2), coli[:, :, :]).then_inc(table_out, 16)
            sp.wait_ge(table_out, 16)
            sp.dma_start(k.table[0:1, :], k.table_d.rearrange("w f -> (w f)").rearrange("(a n) -> a n", a=1)
                         ).then_inc(table_in, 16)
            sp.wait_ge(table_in, 16)
            sp.wait_ge(x_in, 32)

        @block.gpsimd
        def _(pool):
            pool.memset(dst_i[:, ECT - 1, :], -1).then_inc(pool_done, 1)
            pool.memset(src_i[:, ECT - 1, :], -1).then_inc(pool_done, 1)
            pool.memset(ew[:, ECT - 1, :], 0.0).then_inc(pool_done, 1)
            pool.memset(k.X[:, NT - 1, :], 0.0).then_inc(pool_done, 1)
            pool.iota(cidx_i[:, :], pattern=[[P, ECT]], base=0, channel_multiplier=1).then_inc(pool_done, 1)
            pool.iota(win_i[:, :], pattern=[[WD, NW]], base=0, channel_multiplier=0).then_inc(pool_done, 1)
            pool.memset(k.ident[:, :], 0.0).then_inc(pool_done, 1)
            pool.memset(ones[:, :], 1.0).then_inc(pool_done, 1)
            pool.memset(k.zeros[:, :], 0.0).then_inc(pool_done, 1)
            pool.iota(k.iota_low[:, :], pattern=[[1, SL]], base=0, channel_multiplier=0).then_inc(pool_done, 1)
            pool.iota(k.iota_key[:, :], pattern=[[1, P]], base=0, channel_multiplier=0).then_inc(pool_done, 1)
            pool.iota(base_i[:, :], pattern=[[P, NW]], base=0, channel_multiplier=0).then_inc(pool_done, 1)
            pool.wait_ge(pool_done, 12)
            pool.affine_select(out=k.ident[:, :], in_=k.ident[:, :], compare_op=ALU.not_equal, fill=1.0,
                               base=0, pattern=[[-1, P]], channel_multiplier=1).then_inc(pool_done, 1)
            pool.affine_select(out=tri[:, :], in_=ones[:, :], compare_op=ALU.is_gt, fill=0.0,
                               base=0, pattern=[[1, HW_]], channel_multiplier=-1).then_inc(pool_done, 1)

        @block.vector
        def _(dve):
            count = [0]

            def step(ins):
                count[0] += 1
                ins.then_inc(dve_done, 1)
                dve.wait_ge(dve_done, count[0])

            dve.wait_ge(pool_done, 14)
            dve.wait_ge(loaded, 9 * 16)
            step(dve.tensor_copy(dst[:], dst_i[:]))
            step(dve.tensor_copy(src[:], src_i[:]))
            step(dve.tensor_scalar(hi[:], src[:], float(SL), None, ALU.is_ge))
            for s in range(2, NSH):
                step(dve.scalar_tensor_tensor(hi[:], src[:], float(SL * s), hi[:], ALU.is_ge, ALU.add))
            step(dve.scalar_tensor_tensor(rows[:, 0], dst[:], float(NSH), hi[:], ALU.mult, ALU.add))
            step(dve.scalar_tensor_tensor(rows[:, 1], hi[:], -float(SL), src[:], ALU.mult, ALU.add))
            step(dve.tensor_copy(part_b[:], ew[:]))
            step(dve.tensor_copy(rows[:, 2], part_b[:]))
            step(dve.tensor_tensor(left[:], ew[:], rows[:, 2], ALU.subtract))
            step(dve.tensor_copy(part_b[:], left[:]))
            step(dve.tensor_copy(rows[:, 3], part_b[:]))
            dve.tensor_tensor(rows[:, 4], left[:], rows[:, 3], ALU.subtract).then_inc(rows_ready, 1)
            step(dve.tensor_scalar(tmp[:], dst[:], 0.0, 1.0e6, ALU.is_lt, ALU.mult))
            step(dve.tensor_tensor(tmp[:], tmp[:], dst[:], ALU.add))
            step(dve.tensor_reduce(cmax[:], dst[:], AX_X, ALU.max))
            step(dve.tensor_reduce(cmin[:], tmp[:], AX_X, ALU.min))
            step(dve.tensor_scalar(cmin[:], cmin[:], -float(WD - 1), None, ALU.add))
            step(dve.tensor_copy(win[:], win_i[:]))
            step(dve.tensor_copy(k.key_base[:], base_i[:]))
            step(dve.tensor_copy(cidx[:], cidx_i[:]))
            step(dve.tensor_scalar(crev[:], cidx[:], -1.0, 1024.0, ALU.mult, ALU.add))
            step(dve.tensor_scalar(cidx[:], cidx[:], 1.0, None, ALU.add))
            step(dve.memset(rng[:], 0.0))
            for t in range(ECT):
                for s, index in ((0, cidx), (1, crev)):
                    step(dve.tensor_scalar(pick[:], win[:], cmin[:, t:t + 1], index[:, t:t + 1],
                                           ALU.is_ge, ALU.mult))
                    step(dve.scalar_tensor_tensor(pick[:], win[:], cmax[:, t:t + 1], pick[:],
                                                  ALU.is_le, ALU.mult))
                    step(dve.tensor_tensor(rng[:, s], rng[:, s], pick[:], ALU.max))
            count[0] += 1
            dve.memset(tmp[:, 0, 0:1], 0.0).then_inc(dve_done, 1)
            dve.wait_ge(dve_done, count[0])
            dve.sem_inc(rng_ready, 1)
            dve.wait_ge(rng_turned, 1)
            step(dve.tensor_reduce(ends[:], ps[0:HW_, 4, 0:4 * P].rearrange("p (a b) -> p a b", a=4), AX_X, ALU.max))
            step(dve.tensor_scalar(first[:], ends[:, 2:4], -1.0, 1024.0, ALU.mult, ALU.add))
            step(dve.tensor_scalar(first[:], first[:], float(NCH), None, ALU.min))
            step(dve.tensor_tensor(span[:], ends[:, 0:2], first[:], ALU.subtract))
            step(dve.tensor_scalar(span[:], span[:], 0.5, 0.25, ALU.mult, ALU.add))
            step(dve.tensor_copy(pairs_i[:], span[:]))
            step(dve.tensor_copy(pairs[:], pairs_i[:]))
            step(dve.tensor_scalar(pairs[:], pairs[:], 2.0, None, ALU.max))
            dve.sem_inc(pairs_ready, 1)
            dve.wait_ge(summed, 1)
            step(dve.tensor_copy(colf[:, :, 0], ps[0:HW_, 5, 0:2]))
            step(dve.tensor_tensor(colf[:, :, 1], colf[:, :, 0], pairs[:], ALU.add))
            step(dve.scalar_tensor_tensor(colf[:, :, 2], colf[:, :, 0], -2.0, first[:], ALU.mult, ALU.add))
            dve.tensor_copy(coli[:], colf[:]).then_inc(cols_ready, 1)

        @block.tensor
        def _(pe):
            pe.wait_ge(pool_done, 14)
            pe.wait_ge(rows_ready, 1)
            for a in range(5):
                if a >= 2:
                    pe.wait_ge(taken, a - 1)
                for t in range(ECT):
                    last = pe.transpose(ps[:, 2 * (a % 2) + t // 4, (t % 4) * P:(t % 4 + 1) * P],
                                        rows[:, a, t, :], k.ident[:, :])
                last.then_inc(turned, 1)
            pe.wait_ge(rng_ready, 1)
            for s in range(4):
                last = pe.transpose(ps[0:HW_, 4, s * P:(s + 1) * P],
                                    rng[:, s // 2, (s % 2) * HW_:(s % 2 + 1) * HW_], k.ident[:, :])
            last.then_inc(rng_turned, 1)
            pe.wait_ge(pairs_ready, 1)
            pe.matmul(ps[0:HW_, 5, 0:2], tri[:, :], pairs[:, :], start=True, stop=True)
            pe.matmul(ps[0:HW_, 5, 1:2], ones[:, :], pairs[:, 0:1], start=False, stop=True,
                      skip_group_check=True).then_inc(summed, 1)

        @block.scalar
        def _(act):
            for a in range(5):
                act.wait_ge(turned, a + 1)
                act.activation(k.cols[:, a, 0:4 * P], ps[:, 2 * (a % 2), :], ACT.Copy)
                act.activation(k.cols[:, a, 4 * P:ECOL], ps[:, 2 * (a % 2) + 1, 0:ECOL - 4 * P], ACT.Copy
                               ).then_inc(taken, 1)


def build_matrices(nc, k):
    with ExitStack() as ctx:
        KEY = ctx.enter_context(nc.sbuf_tensor("KEY", [P, 4, P], BF16))
        OH = ctx.enter_context(nc.sbuf_tensor("OH", [P, 4, 4, SL], BF16))
        stage = ctx.enter_context(nc.sbuf_tensor("stage", [P, 2, 2, SL], F32))
        ps = ctx.enter_context(nc.psum_tensor("ps_build", [P, 4, BANK], F32))
        onehots = ctx.enter_context(nc.semaphore("onehots"))
        third = ctx.enter_context(nc.semaphore("third"))
        used = ctx.enter_context(nc.semaphore("used"))
        copied = ctx.enter_context(nc.semaphore("copied"))
        stored = [ctx.enter_context(nc.semaphore(f"stored{s}")) for s in range(2)]
        ready = ctx.enter_context(nc.semaphore("primed"))
        block = ctx.enter_context(nc.Block())
        WHY = "the table's ranges lie inside the columns"

        def window(eng, w):
            first = eng.value_load(k.table[0:1, bass.ds(w * 3, 1)], min_val=0, max_val=NW * ECOL)
            end = eng.value_load(k.table[0:1, bass.ds(w * 3 + 1, 1)], min_val=2, max_val=NW * ECOL)
            return first, end

        def shift_of(eng, w):
            return eng.value_load(k.table[0:1, bass.ds(w * 3 + 2, 1)], min_val=-2 * NW * ECOL, max_val=NCH)

        def chunk(eng, pair, shift, j):
            return nc.s_assert_within(eng.snap(pair * 2 + (shift + j)), 0, ECOL - 1,
                                      skip_runtime_bounds_check_because=WHY)

        @block.vector
        def _(dve):
            def pair_step(w, pair, shift):
                for j in range(2):
                    c = chunk(dve, pair, shift, j)
                    slot = dve.snap((pair % 2) * 2 + j)
                    dve.wait_ge(used, pair * 2 + (j + 1))
                    dve.tensor_scalar(OH[:, bass.ds(slot, 1), 0, :], k.iota_low[:, :].unsqueeze(1),
                                      k.cols[:, 1, bass.ds(c, 1)], None, ALU.is_equal)
                    dve.tensor_scalar(KEY[:, bass.ds(slot, 1), :], k.iota_key[:, :].unsqueeze(1),
                                      k.key_base[:, bass.ds(w, 1)], k.cols[:, 0, bass.ds(c, 1)],
                                      ALU.add, ALU.is_equal)
                    for v in (1, 2):
                        last = dve.tensor_scalar(OH[:, bass.ds(slot, 1), v, :], k.iota_low[:, :].unsqueeze(1),
                                                 k.cols[:, 1, bass.ds(c, 1)], k.cols[:, 1 + v, bass.ds(c, 1)],
                                                 ALU.is_equal, ALU.mult)
                    last.then_inc(onehots, 1)

            with dve.Fori(0, NW) as w:
                first, end = window(dve, w)
                shift = shift_of(dve, w)
                with dve.Fori(first, end) as pair:
                    pair_step(w, pair, shift)

        @block.scalar
        def _(act):
            def third_part(pair, shift):
                for j in range(2):
                    c = chunk(act, pair, shift, j)
                    slot = act.snap((pair % 2) * 2 + j)
                    act.wait_ge(onehots, pair * 2 + (j + 1))
                    act.activation(OH[:, bass.ds(slot, 1), 3, :], OH[:, bass.ds(slot, 1), 0, :], ACT.Copy,
                                   scale=k.cols[:, 4, bass.ds(c, 1)]).then_inc(third, 1)

            def copy_out(w, slot, end):
                act.wait_ge(used, end * 2 + 4)
                if slot is not None:
                    act.wait_ge(stored[slot], w * 16 + 16)
                act.activation(stage[:, slot], ps[:, 2 * slot:2 * slot + 2, 0:SL], ACT.Copy).then_inc(copied, 1)

            for s in range(2):
                act.sem_inc(stored[s], 16)
            with act.Fori(0, HW_) as w2:
                for s in range(2):
                    w = w2 * 2 + s
                    first, end = window(act, w)
                    shift = shift_of(act, w)
                    with act.Fori(first, end) as pair:
                        third_part(pair, shift)
                    copy_out(w2, s, end)

        @block.tensor
        def _(pe):
            pe.sem_inc(used, 4)
            pe.sem_inc(copied, 2)

            def products(pair, s, j, start):
                slot = pe.snap((pair % 2) * 2 + j)
                pe.wait_ge(third, pair * 2 + (j + 1))
                for v in range(4):
                    last = pe.matmul(ps[:, 2 * s + (v > 0), 0:SL], KEY[:, slot, :], OH[:, slot, v, :],
                                     start=start and v < 2, stop=True, skip_group_check=True)
                last.then_inc(used, 1)

            with pe.Fori(0, HW_) as w2:
                for s in range(2):
                    w = w2 * 2 + s
                    first, end = window(pe, w)
                    pe.wait_ge(copied, w + 1)
                    products(first, s, 0, True)
                    products(first, s, 1, False)
                    with pe.Fori(first + 1, end) as pair:
                        products(pair, s, 0, False)
                        products(pair, s, 1, False)

        @block.sync
        def _(sp):
            with sp.Fori(0, HW_) as w2:
                for s in range(2):
                    w = w2 * 2 + s
                    sp.wait_ge(copied, w + 3)
                    sp.dma_start(k.adj_w[bass.ds(w, 1)].rearrange("w p v c -> p (w v) c"), stage[:, s]
                                 ).then_inc(stored[s], 16)
            for s in range(2):
                sp.wait_ge(stored[s], HW_ * 16 + 16)


def tile_columns(t, width=D, per_bank=4):
    return t // per_bank, (t % per_bank) * width


def flat(ps, columns=NP):
    return ps[:, :, :].rearrange("p b c -> p (b c)")[:, 0:columns]


def tiles_of(ps):
    return flat(ps).rearrange("p (t d) -> p t d", d=D)


def project(pe, ps, left, weights):
    for t in range(NT):
        b, c = tile_columns(t)
        for n, (lt, w) in enumerate(zip(left, weights)):
            last = pe.matmul(ps[:, b, c:c + D], lt[:, t * P:(t + 1) * P], w, start=n == 0, stop=True,
                             skip_group_check=n > 0)
    return last


def turn(pe, ps, nodes, ident):
    for t in range(NT):
        b, c = tile_columns(t)
        last = pe.transpose(ps[:, b, c:c + P], nodes[:, t, :], ident)
    return last


def turn_back(pe, ps, feats, ident):
    for t in range(NT):
        b, c = tile_columns(t)
        last = pe.transpose(ps[:, b, c:c + P], feats[:, t * P:(t + 1) * P], ident)
    return last


def hold(eng, sem, value, held):
    eng.wait_ge(sem, value)
    eng.sem_inc(held, 1)


class Chain:

    def __init__(self, eng, sem):
        self.eng, self.sem, self.n = eng, sem, 0

    def step(self, ins):
        self.n += 1
        ins.then_inc(self.sem, 1)
        self.eng.wait_ge(self.sem, self.n)


def normalise(dve, ch, b, src, dst, var_ready, root_ready, n):
    for t in range(NT):
        last = dve.bn_stats(b.s6[:, t, :], src[:, t, :])
    ch.step(last)
    ch.step(dve.tensor_tensor(b.mean[:], b.s6[:, :, 1], b.s6[:, :, 4], ALU.add))
    ch.step(dve.tensor_tensor(b.dif[:], b.s6[:, :, 1], b.s6[:, :, 4], ALU.subtract))
    ch.step(dve.tensor_tensor(b.dif[:], b.dif[:], b.dif[:], ALU.mult))
    ch.step(dve.tensor_tensor(b.var[:], b.s6[:, :, 2], b.s6[:, :, 5], ALU.add))
    ch.step(dve.scalar_tensor_tensor(b.var[:], b.dif[:], D / 4.0, b.var[:], ALU.mult, ALU.add))
    ch.step(dve.tensor_scalar(b.mean[:], b.mean[:], 0.5, None, ALU.mult))
    dve.tensor_scalar(b.var[:], b.var[:], 1.0 / D, EPS_LN, ALU.mult, ALU.add).then_inc(var_ready, 1)
    dve.wait_ge(root_ready, n)
    ch.step(dve.reciprocal(b.root[:], b.root[:]))
    wide = [P, NT, D]
    ch.step(dve.tensor_tensor(dst, src, b.mean[:].unsqueeze(2).to_broadcast(wide), ALU.subtract))
    ch.step(dve.tensor_tensor(dst, dst, b.root[:].unsqueeze(2).to_broadcast(wide), ALU.mult))


def root(act, b, var_ready, root_ready, n):
    act.wait_ge(var_ready, n)
    act.activation(b.root[:], b.var[:], ACT.Sqrt).then_inc(root_ready, 1)


def aggregate(nc, k, name, matrix, nodes, out_t):
    with ExitStack() as ctx:
        ring = ctx.enter_context(nc.sbuf_tensor(f"{name}_ring", [P, UN, NP], F32))
        left = ctx.enter_context(nc.sbuf_tensor(f"{name}_left", [P, UN, D], F32))
        ps = ctx.enter_context(nc.psum_tensor(f"{name}_ps", [P, 8, BANK], F32))
        loaded = [ctx.enter_context(nc.semaphore(f"{name}_loaded{u}")) for u in range(UN)]
        left_ready = ctx.enter_context(nc.semaphore(f"{name}_left_ready"))
        used = ctx.enter_context(nc.semaphore(f"{name}_used"))
        block = ctx.enter_context(nc.Block())
        rows = matrix.rearrange("(t p) c -> t p c", p=P)

        @block.sync
        def _(sp):
            with sp.Fori(0, NT // UN) as lap:
                for u in range(UN):
                    t = lap * UN + u
                    sp.wait_ge(used, t + 1)
                    sp.dma_start(ring[:, u, :].unsqueeze(1), rows[bass.ds(t, 1)].rearrange("t p c -> p t c")
                                 ).then_inc(loaded[u], 16)

        @block.gpsimd
        def _(pool):
            with pool.Fori(0, NT // UN) as lap:
                for u in range(UN):
                    t = lap * UN + u
                    pool.wait_ge(used, t + 1)
                    pool.tensor_copy(left[:, u, :].unsqueeze(1), nodes[:, bass.ds(t, 1), :]).then_inc(left_ready, 1)

        @block.tensor
        def _(pe):
            for b in range(NCW):
                last = pe.matmul(ps[:, b, 0:CW], k.zeros[:, 0:P], k.zeros[:, 0:CW], start=True, stop=True)
            pe.sem_inc(used, UN)
            with pe.Fori(0, NT // UN) as lap:
                for u in range(UN):
                    pe.wait_ge(loaded[u], lap * 16 + 16)
                    pe.wait_ge(left_ready, lap * UN + (u + 1))
                    for b in range(NCW):
                        last = pe.matmul(ps[:, b, 0:CW], left[:, u, :], ring[:, u, b * CW:(b + 1) * CW],
                                         start=False, stop=True, skip_group_check=True)
                    last.then_inc(used, 1)

        @block.scalar
        def _(act):
            act.wait_ge(used, UN + NT)
            act.activation(out_t[:, 0:HALF].rearrange("p (b c) -> p b c", c=CW), ps[:, 0:HB, 0:CW], ACT.Copy)

        @block.vector
        def _(dve):
            dve.wait_ge(used, UN + NT)
            dve.tensor_copy(out_t[:, HALF:NP].rearrange("p (b c) -> p b c", c=CW), ps[:, HB:NCW, 0:CW])


def finish_gcn(nc, k, agg):
    with ExitStack() as ctx:
        def sb(name, shape, dt=F32):
            return ctx.enter_context(nc.sbuf_tensor(name, shape, dt))

        def sem(name):
            return ctx.enter_context(nc.semaphore(name))

        w = sb("gcn_w", [D, D])
        bias = sb("gcn_bias", [P, D])
        T = sb("gcn_t", [P, NT, D])
        b = NormBuffers(sb, "gcn")
        ps = ctx.enter_context(nc.psum_tensor("gcn_ps", [P, 8, BANK], F32))
        loaded, projected, chain, var_ready, root_ready, x_ready, x_turned = map(
            sem, ("gcn_loaded", "gcn_projected", "gcn_chain", "gcn_var", "gcn_root", "gcn_x", "gcn_turned"))
        block = ctx.enter_context(nc.Block())

        @block.sync
        def _(sp):
            sp.dma_start(w[:], k.L0_gnn_weight).then_inc(loaded, 16)
            sp.dma_start(bias[:], k.L0_gnn_b.partition_broadcast(P)).then_inc(loaded, 16)

        @block.tensor
        def _(pe):
            pe.wait_ge(loaded, 32)
            project(pe, ps, [agg], [w[:]]).then_inc(projected, 1)
            pe.wait_ge(x_ready, 1)
            turn(pe, ps, k.X, k.ident[:]).then_inc(x_turned, 1)

        @block.vector
        def _(dve):
            ch = Chain(dve, chain)
            dve.wait_ge(projected, 1)
            ch.step(dve.tensor_tensor(T[:], tiles_of(ps), bias[:].unsqueeze(1).to_broadcast([P, NT, D]), ALU.add))
            ch.step(dve.scalar_tensor_tensor(T[:], T[:], 0.0, k.X[:], ALU.max, ALU.add))
            normalise(dve, ch, b, T[:], k.X[:], var_ready, root_ready, 1)
            dve.sem_inc(x_ready, 1)

        @block.scalar
        def _(act):
            root(act, b, var_ready, root_ready, 1)
            act.wait_ge(x_turned, 1)
            act.activation(k.XT[:], flat(ps), ACT.Copy)


def gat_project(nc, k, heads, cols, rows_d):
    with ExitStack() as ctx:
        def sb(name, shape, dt=F32):
            return ctx.enter_context(nc.sbuf_tensor(name, shape, dt))

        def sem(name):
            return ctx.enter_context(nc.semaphore(name))

        w = sb("gat_w", [D, D])
        att = sb("gat_att", [P, 2, HEADS, C])
        mixed = sb("gat_mixed", [P, 2, HEADS, C])
        watt = sb("gat_watt", [P, 2 * HEADS])
        rows = sb("gat_rows", [2 * HEADS, NP])
        ps = ctx.enter_context(nc.psum_tensor("gatp_ps", [P, 8, BANK], F32))
        loaded, ones, watt_ready, projected, copied, rows_made, rows_copied, stored = map(
            sem, ("gp_loaded", "gp_ones", "gp_watt", "gp_projected", "gp_copied", "gp_rows", "gp_rows_copied",
                  "gp_stored"))
        chain = sem("gp_chain")
        block = ctx.enter_context(nc.Block())

        @block.sync
        def _(sp):
            sp.dma_start(w[:], k.L1_gnn_W).then_inc(loaded, 16)
            for s, a in ((0, k.L1_gnn_att_src), (1, k.L1_gnn_att_dst)):
                sp.dma_start(att[:, s].rearrange("p h c -> p (h c)"), a.rearrange("h c -> (h c)").partition_broadcast(P)
                             ).then_inc(loaded, 16)
            sp.wait_ge(rows_copied, 2)
            sp.dma_start(rows_d, rows[:]).then_inc(stored, 16)
            sp.wait_ge(stored, 16)

        @block.gpsimd
        def _(pool):
            pool.memset(heads[:], 1.0).then_inc(ones, 1)

        @block.tensor
        def _(pe):
            pe.wait_ge(loaded, 48)
            project(pe, ps, [k.XT], [w[:]]).then_inc(projected, 1)
            pe.wait_ge(watt_ready, 1)
            for t in range(NT):
                last = pe.matmul(ps[:, 7, t * 8:(t + 1) * 8], k.XT[:, t * P:(t + 1) * P], watt[:], start=True,
                                 stop=True, skip_group_check=True)
            last.then_inc(projected, 1)
            pe.wait_ge(copied, 2)
            for b in range(NCW):
                last = pe.matmul(ps[0:8, b, 0:CW], watt[:], k.XT[:, b * CW:(b + 1) * CW], start=True, stop=True)
            last.then_inc(rows_made, 1)

        @block.vector
        def _(dve):
            ch = Chain(dve, chain)
            dve.wait_ge(loaded, 48)
            for s in range(2):
                ch.step(dve.tensor_tensor(mixed[:, s], w[:].rearrange("p (h c) -> p h c", c=C), att[:, s], ALU.mult))
            dve.tensor_reduce(watt[:], mixed[:].rearrange("p s h c -> p (s h) c"), AX_X, ALU.add
                              ).then_inc(watt_ready, 1)
            dve.wait_ge(projected, 2)
            dve.tensor_copy(cols[:].rearrange("p k t -> p t k"),
                            ps[:, 7, 0:8 * NT].rearrange("p (t k) -> p t k", k=8)).then_inc(copied, 1)
            dve.wait_ge(rows_made, 1)
            dve.tensor_copy(rows[:, HALF:NP].rearrange("p (b c) -> p b c", c=CW), ps[0:8, HB:NCW, 0:CW]
                            ).then_inc(rows_copied, 1)

        @block.scalar
        def _(act):
            act.wait_ge(projected, 1)
            act.wait_ge(ones, 1)
            for h in range(HEADS):
                last = act.activation(heads[:, h, :, 0:C], tiles_of(ps)[:, :, h * C:(h + 1) * C], ACT.Copy)
            last.then_inc(copied, 1)
            act.wait_ge(rows_made, 1)
            act.activation(rows[:, 0:HALF].rearrange("p (b c) -> p b c", c=CW), ps[0:8, 0:HB, 0:CW], ACT.Copy
                           ).then_inc(rows_copied, 1)


def gat_max(nc, k, rows_d, best):
    with ExitStack() as ctx:
        def sb(name, shape, dt=F32):
            return ctx.enter_context(nc.sbuf_tensor(name, shape, dt))

        def sem(name):
            return ctx.enter_context(nc.semaphore(name))

        ring = sb("gm_ring", [P, UN, NP])
        src_rows = sb("gm_src_rows", [P, HEADS, NP])
        closed = sb("gm_closed", [P, NP], BF16)
        unread = sb("gm_unread", [P, HEADS, NP], BF16)
        best_u = sb("gm_best_u", [P, UN, HEADS])
        turned_sb = sb("gm_turned", [P, NT, P])
        ps = ctx.enter_context(nc.psum_tensor("gm_ps", [P, 8, BANK], F32))
        rows_in, held, maxed = sem("gm_rows_in"), sem("gm_held"), sem("gm_maxed")
        loaded = [sem(f"gm_loaded{u}") for u in range(UN)]
        turned, copied, masked, best_set, stored, chain = map(
            sem, ("gm_turned_s", "gm_copied", "gm_masked", "gm_best", "gm_stored", "gm_chain"))
        block = ctx.enter_context(nc.Block())
        rows = k.count_rs.rearrange("(t p) c -> t p c", p=P)
        cols_out = k.count_sr.rearrange("(b p) (t c) -> t p b c", p=P, c=P)

        @block.sync
        def _(sp):
            for h in range(HEADS):
                sp.dma_start(src_rows[:, h], rows_d[h].partition_broadcast(P)).then_inc(rows_in, 16)
            with sp.Fori(0, NT // UN) as lap:
                for u in range(UN):
                    t = lap * UN + u
                    sp.wait_ge(turned, t + 1)
                    sp.wait_ge(masked, t + 1)
                    sp.dma_start(ring[:, u, :].unsqueeze(1), rows[bass.ds(t, 1)].rearrange("t p c -> p t c")
                                 ).then_inc(loaded[u], 16)

        @block.tensor
        def _(pe):
            pe.sem_inc(turned, UN)
            with pe.Fori(0, NT // UN) as lap:
                for u in range(UN):
                    pe.wait_ge(loaded[u], lap * 16 + 16)
                    pe.wait_ge(copied, lap * UN + (u + 1))
                    for s in range(NT):
                        b, c = tile_columns(s)
                        last = pe.transpose(ps[:, b, c:c + P], ring[:, u, s * P:(s + 1) * P], k.ident[:])
                    last.then_inc(turned, 1)

        @block.scalar
        def _(act):
            act.sem_inc(copied, 1)
            act.sem_inc(stored, 16)
            with act.Fori(0, NT // UN) as lap:
                for u in range(UN):
                    t = lap * UN + u
                    act.wait_ge(stored, t * 16 + 16)
                    act.wait_ge(turned, t + (UN + 1))
                    act.activation(turned_sb[:].rearrange("p t c -> p (t c)"), flat(ps), ACT.Copy).then_inc(copied, 1)
                    act.wait_ge(copied, t + 2)
                    act.dma_start(cols_out[bass.ds(t, 1)].rearrange("t p b c -> p (t b) c"), turned_sb[:]
                                  ).then_inc(stored, 16)
            act.wait_ge(stored, NT * 16 + 16)

        @block.vector
        def _(dve):
            dve.sem_inc(masked, UN)
            dve.sem_inc(maxed, 1)
            dve.wait_ge(rows_in, HEADS * 16)
            with dve.Fori(0, NT // UN) as lap:
                for u in range(UN):
                    t = lap * UN + u
                    dve.wait_ge(loaded[u], lap * 16 + 16)
                    dve.wait_ge(maxed, t + 1)
                    dve.tensor_scalar(closed[:], ring[:, u, :], 0.0, -BIG, ALU.is_equal, ALU.mult).then_inc(masked, 1)
                    hold(dve, masked, t + (UN + 1), held)
                    for h in range(HEADS):
                        last = dve.tensor_tensor_reduce(out=unread[:, h], in0=closed[:], in1=src_rows[:, h], scale=1.0,
                                                        scalar=-3.0e38, op0=ALU.add, op1=ALU.max,
                                                        accum_out=best_u[:, u, h:h + 1])
                    last.then_inc(maxed, 1)
                dve.wait_ge(maxed, lap * UN + (UN + 1))
                dve.tensor_copy(best[:, :, bass.ds(lap * UN, UN)], best_u[:].rearrange("p u h -> p h u")
                                ).then_inc(chain, 1)
                dve.wait_ge(chain, lap + 1)


def gat_exponents(nc, k, cols, best, own, u_d):
    with ExitStack() as ctx:
        def sb(name, shape, dt=F32):
            return ctx.enter_context(nc.sbuf_tensor(name, shape, dt))

        def sem(name):
            return ctx.enter_context(nc.semaphore(name))

        z = sb("ge_z", [P, HEADS, NT])
        m = sb("ge_m", [P, HEADS, NT])
        u = sb("ge_u", [P, 2, HEADS, NT])
        ut = sb("ge_ut", [HEADS * NT, 2, P])
        ps = ctx.enter_context(nc.psum_tensor("ge_ps", [P, 1, BANK], F32))
        chain, turned, copied, stored = map(sem, ("ge_chain", "ge_turned", "ge_copied", "ge_stored"))
        u_ready, own_ready = sem("ge_u_ready"), sem("ge_own_ready")
        block = ctx.enter_context(nc.Block())

        @block.scalar
        def _(act):
            act.wait_ge(own_ready, 1)
            act.activation(own[:], own[:], ACT.Exp)

        @block.vector
        def _(dve):
            ch = Chain(dve, chain)
            a_d = cols[:, HEADS:2 * HEADS]
            ch.step(dve.tensor_tensor(best[:], best[:], cols[:, 0:HEADS], ALU.max))
            ch.step(dve.tensor_tensor(z[:], best[:], a_d, ALU.add))
            ch.step(dve.scalar_tensor_tensor(m[:], z[:], 0.2, z[:], ALU.mult, ALU.max))
            ch.step(dve.tensor_tensor(u[:, 0], a_d, m[:], ALU.subtract))
            ch.step(dve.scalar_tensor_tensor(u[:, 1], a_d, 0.2, m[:], ALU.mult, ALU.subtract))
            ch.step(dve.tensor_tensor(z[:], cols[:, 0:HEADS], a_d, ALU.add))
            ch.step(dve.scalar_tensor_tensor(z[:], z[:], 0.2, z[:], ALU.mult, ALU.max))
            dve.tensor_tensor(own[:], z[:], m[:], ALU.subtract).then_inc(own_ready, 1)
            dve.tensor_scalar(cols[:, HEADS:2 * HEADS], cols[:, 0:HEADS], 0.2, None, ALU.mult).then_inc(u_ready, 1)
            dve.wait_ge(turned, 1)
            dve.tensor_copy(ut[:].rearrange("p a b -> p (a b)"), ps[0:HEADS * NT, 0, 0:2 * P]).then_inc(copied, 1)

        @block.tensor
        def _(pe):
            pe.wait_ge(u_ready, 1)
            for s in range(2):
                last = pe.transpose(ps[0:HEADS * NT, 0, s * P:(s + 1) * P], u[:, s].rearrange("p h t -> p (h t)"),
                                    k.ident[:])
            last.then_inc(turned, 1)

        @block.sync
        def _(sp):
            sp.wait_ge(copied, 1)
            sp.dma_start(u_d.rearrange("(s h) (t p) -> (h t) s p", s=2, p=P), ut[:]).then_inc(stored, 16)
            sp.wait_ge(stored, 16)


def gat_attend(nc, k, heads, cols, u_d, sums_d):
    with ExitStack() as ctx:
        def sb(name, shape, dt=F32):
            return ctx.enter_context(nc.sbuf_tensor(name, shape, dt))

        def sem(name):
            return ctx.enter_context(nc.semaphore(name))

        count = sb("ga_count", [P, UN, HALF])
        p = sb("ga_p", [P, UN, HALF])
        u = sb("ga_u", [P, 2, 2, HALF])
        left = sb("ga_left", [P, UN, C + 1])
        sums = sb("ga_sums", [C + 1, 2, HALF])
        ps = ctx.enter_context(nc.psum_tensor("ga_ps", [P, 8, BANK], F32))
        loaded = [sem(f"ga_loaded{s}") for s in range(UN)]
        u_in = [sem(f"ga_u_in{s}") for s in range(2)]
        stored = [sem(f"ga_stored{s}") for s in range(2)]
        read = sem("ga_read")
        slopes, larger, scores, exps, probs, left_ready, used, copied = map(
            sem, ("ga_slopes", "ga_larger", "ga_scores", "ga_exps", "ga_probs", "ga_left_ready", "ga_used", "ga_copied"))
        block = ctx.enter_context(nc.Block())
        rows = k.count_sr.rearrange("(t p) (s c) -> t s p c", p=P, s=2)
        u_rows = u_d.rearrange("(r h) (s c) -> h s r c", r=2, s=2)
        out_rows = sums_d.rearrange("h f (s c) -> h s f c", s=2)
        UNITS = NT

        @block.sync
        def _(sp):
            with sp.Fori(0, HEADS) as h:
                for s in range(2):
                    sp.wait_ge(read, h * 2 + (s + 1))
                    sp.dma_start(u[:, s], u_rows[bass.ds(h, 1), s].rearrange("h r c -> (h r) c").partition_broadcast(P)
                                 ).then_inc(u_in[s], 16)
                    with sp.Fori(0, NT // UN) as lap:
                        for n in range(UN):
                            t = lap * UN + n
                            sp.wait_ge(used, (h * 2 + s) * UNITS + t + 1)
                            sp.dma_start(count[:, n, :].unsqueeze(1), rows[bass.ds(t, 1), s].rearrange("t p c -> p t c")
                                         ).then_inc(loaded[n], 16)

        @block.gpsimd
        def _(pool):
            with pool.Fori(0, HEADS) as h:
                for s in range(2):
                    with pool.Fori(0, NT // UN) as lap:
                        for n in range(UN):
                            t = lap * UN + n
                            pool.wait_ge(used, (h * 2 + s) * UNITS + t + 1)
                            pool.tensor_copy(left[:, n, :].unsqueeze(1).unsqueeze(1),
                                             heads[:, bass.ds(h, 1), bass.ds(t, 1), :]).then_inc(left_ready, 1)

        @block.scalar
        def _(act):
            act.sem_inc(copied, 2)
            for s in range(2):
                act.sem_inc(stored[s], 16)
            with act.Fori(0, HEADS) as h:
                for s in range(2):
                    base = (h * 2 + s) * UNITS
                    act.wait_ge(u_in[s], h * 16 + 16)

                    def slope(lap, n):
                        t = lap * UN + n
                        act.wait_ge(used, base + t + 1)
                        act.activation(p[:, n, :], u[:, s, 1], ACT.Identity,
                                       bias=cols[:, bass.ds(h + HEADS, 1), bass.ds(t, 1)].rearrange("p a b -> p (a b)")
                                       ).then_inc(slopes, 1)

                    with act.Fori(0, NT // UN) as lap:
                        slope(lap, 0)
                        slope(lap, 1)
                        for n in range(UN):
                            act.wait_ge(scores, base + lap * UN + (n + 1))
                            act.activation(p[:, n, :], p[:, n, :], ACT.Exp).then_inc(exps, 1)
                            if n + 2 < UN:
                                slope(lap, n + 2)
                    act.wait_ge(used, base + (UNITS + UN))
                    act.wait_ge(stored[s], h * 16 + 16)
                    act.activation(sums[:, s].rearrange("p (b c) -> p b c", c=CW),
                                   ps[0:C + 1, s * HB:(s + 1) * HB, 0:CW], ACT.Copy).then_inc(copied, 1)
                    act.wait_ge(copied, h * 2 + (s + 3))
                    act.dma_start(out_rows[bass.ds(h, 1), s].rearrange("h f c -> f h c"), sums[:, s, :].unsqueeze(1)
                                  ).then_inc(stored[s], 16)
            for s in range(2):
                act.wait_ge(stored[s], HEADS * 16 + 16)

        @block.vector
        def _(dve):
            dve.sem_inc(read, 2)
            with dve.Fori(0, HEADS) as h:
                for s in range(2):
                    base = (h * 2 + s) * UNITS

                    def prob(lap, n):
                        t = lap * UN + n
                        dve.wait_ge(exps, base + t + 1)
                        dve.wait_ge(loaded[n], (h * 2 + s) * (16 * (NT // UN)) + lap * 16 + 16)
                        dve.tensor_tensor(p[:, n, :], p[:, n, :], count[:, n, :], ALU.mult).then_inc(probs, 1)

                    def bound(lap, n):
                        dve.wait_ge(larger, base + lap * UN + (n + 1))
                        dve.tensor_scalar(p[:, n, :], p[:, n, :], 0.0, None, ALU.min).then_inc(scores, 1)

                    with dve.Fori(0, NT // UN) as lap:
                        for n in range(UN):
                            t = lap * UN + n
                            dve.wait_ge(slopes, base + t + 1)
                            dve.scalar_tensor_tensor(
                                p[:, n, :], u[:, s, 0],
                                cols[:, bass.ds(h, 1), bass.ds(t, 1)].rearrange("p a b -> p (a b)"),
                                p[:, n, :], ALU.add, ALU.max).then_inc(larger, 1)
                            if n:
                                bound(lap, n - 1)
                            if n >= 2:
                                prob(lap, n - 2)
                        bound(lap, UN - 1)
                        prob(lap, UN - 2)
                        prob(lap, UN - 1)
                    dve.wait_ge(larger, base + UNITS)
                    dve.sem_inc(read, 1)

        @block.tensor
        def _(pe):
            pe.sem_inc(used, UN)
            with pe.Fori(0, HEADS) as h:
                for s in range(2):
                    base = (h * 2 + s) * UNITS
                    pe.wait_ge(copied, h * 2 + (s + 1))
                    for b in range(HB):
                        pe.matmul(ps[0:C + 1, s * HB + b, 0:CW], k.zeros[:, 0:C + 1], k.zeros[:, 0:CW],
                                  start=True, stop=True)
                    with pe.Fori(0, NT // UN) as lap:
                        for n in range(UN):
                            t = lap * UN + n
                            pe.wait_ge(left_ready, base + t + 1)
                            pe.wait_ge(probs, base + t + 1)
                            for b in range(HB):
                                last = pe.matmul(ps[0:C + 1, s * HB + b, 0:CW], left[:, n, :],
                                                 p[:, n, b * CW:(b + 1) * CW], start=False, stop=True,
                                                 skip_group_check=True)
                            last.then_inc(used, 1)


def finish_gat(nc, k, sums_d, heads, own):
    with ExitStack() as ctx:
        def sb(name, shape, dt=F32):
            return ctx.enter_context(nc.sbuf_tensor(name, shape, dt))

        def sem(name):
            return ctx.enter_context(nc.semaphore(name))

        sums = sb("fg_sums", [C + 1, HEADS, NP])
        node = sb("fg_node", [P, HEADS * NT, C + 1])
        inv = sb("fg_inv", [P, HEADS * NT])
        T = sb("fg_t", [P, NT, D])
        w = sb("fg_w", [D, D])
        vecs = sb("fg_vecs", [P, 4, D])
        b = NormBuffers(sb, "gat")
        ps = ctx.enter_context(nc.psum_tensor("fg_ps", [P, 8, BANK], F32))
        loaded, turned, copied, projected, chain, var_ready, root_ready, x_ready, x_turned = map(
            sem, ("fg_loaded", "fg_turned", "fg_copied", "fg_projected", "fg_chain", "fg_var", "fg_root", "fg_x",
                  "fg_x_turned"))
        block = ctx.enter_context(nc.Block())
        PER = BANK // (C + 1)

        @block.sync
        def _(sp):
            sp.dma_start(sums[:], sums_d.rearrange("h f n -> f h n")).then_inc(loaded, 16)
            sp.dma_start(w[:], k.L1_gnn_skip_W).then_inc(loaded, 16)
            for n, v in enumerate((k.L1_gnn_gat_bias, k.L1_gnn_skip_b, k.L1_gnn_ln_g, k.L1_gnn_ln_b)):
                sp.dma_start(vecs[:, n], v.partition_broadcast(P)).then_inc(loaded, 16)

        @block.tensor
        def _(pe):
            pe.wait_ge(loaded, 96)
            for i in range(HEADS * NT):
                h, t = divmod(i, NT)
                bank, c = tile_columns(i, C + 1, PER)
                last = pe.transpose(ps[:, bank, c:c + C + 1], sums[:, h, t * P:(t + 1) * P], k.ident[0:C + 1, 0:C + 1])
            last.then_inc(turned, 1)
            pe.wait_ge(copied, 1)
            project(pe, ps, [k.XT], [w[:]]).then_inc(projected, 1)
            pe.wait_ge(x_ready, 1)
            turn(pe, ps, k.X, k.ident[:]).then_inc(x_turned, 1)

        @block.scalar
        def _(act):
            act.wait_ge(turned, 1)
            for bank in range(-(-HEADS * NT // PER)):
                n = min(PER, HEADS * NT - bank * PER)
                last = act.activation(node[:, bank * PER:bank * PER + n, :],
                                      ps[:, bank, 0:n * (C + 1)].rearrange("p (n c) -> p n c", c=C + 1), ACT.Copy)
            last.then_inc(copied, 1)
            root(act, b, var_ready, root_ready, 1)
            root(act, b, var_ready, root_ready, 2)
            act.wait_ge(x_turned, 1)
            act.activation(k.XT[:], flat(ps), ACT.Copy)

        @block.vector
        def _(dve):
            ch = Chain(dve, chain)
            wide = [P, NT, D]
            dve.wait_ge(loaded, 96)
            ch.step(dve.tensor_tensor(vecs[:, 0], vecs[:, 0], vecs[:, 1], ALU.add))
            all_heads = heads[:].rearrange("p h t c -> p (h t) c")
            ch.step(dve.tensor_tensor(all_heads, all_heads, own[:].rearrange("p h t -> p (h t)").unsqueeze(2)
                                      .to_broadcast([P, HEADS * NT, C + 1]), ALU.mult))
            dve.wait_ge(copied, 1)
            ch.step(dve.tensor_tensor(node[:], node[:], all_heads, ALU.add))
            ch.step(dve.tensor_scalar(inv[:], node[:, :, C], 1e-16, None, ALU.add))
            ch.step(dve.reciprocal(inv[:], inv[:]))
            for h in range(HEADS):
                ch.step(dve.tensor_tensor(T[:, :, h * C:(h + 1) * C], node[:, h * NT:(h + 1) * NT, 0:C],
                                          inv[:, h * NT:(h + 1) * NT].unsqueeze(2).to_broadcast([P, NT, C]), ALU.mult))
            ch.step(dve.tensor_tensor(T[:], T[:], vecs[:, 0].unsqueeze(1).to_broadcast(wide), ALU.add))
            dve.wait_ge(projected, 1)
            ch.step(dve.tensor_tensor(T[:], T[:], tiles_of(ps), ALU.add))
            normalise(dve, ch, b, T[:], T[:], var_ready, root_ready, 1)
            ch.step(dve.tensor_tensor(T[:], T[:], vecs[:, 2].unsqueeze(1).to_broadcast(wide), ALU.mult))
            ch.step(dve.tensor_tensor(T[:], T[:], vecs[:, 3].unsqueeze(1).to_broadcast(wide), ALU.add))
            ch.step(dve.tensor_tensor(T[:], T[:], k.X[:], ALU.add))
            normalise(dve, ch, b, T[:], k.X[:], var_ready, root_ready, 2)
            dve.sem_inc(x_ready, 1)


def attention_project(nc, k, QT, KT):
    with ExitStack() as ctx:
        wq = ctx.enter_context(nc.sbuf_tensor("ap_wq", [D, D], F32))
        wk = ctx.enter_context(nc.sbuf_tensor("ap_wk", [D, D], F32))
        ps = ctx.enter_context(nc.psum_tensor("ap_ps", [P, 8, BANK], F32))
        loaded = ctx.enter_context(nc.semaphore("ap_loaded"))
        made = ctx.enter_context(nc.semaphore("ap_made"))
        copied = ctx.enter_context(nc.semaphore("ap_copied"))
        block = ctx.enter_context(nc.Block())

        @block.sync
        def _(sp):
            sp.dma_start(wq[:], k.L2_gnn_Wq).then_inc(loaded, 16)
            sp.dma_start(wk[:], k.L2_gnn_Wk).then_inc(loaded, 16)

        @block.tensor
        def _(pe):
            pe.wait_ge(loaded, 32)
            for n, w in enumerate((wq, wk)):
                for b in range(NCW):
                    if n:
                        pe.wait_ge(copied, b + 1)
                    pe.matmul(ps[:, b, 0:CW], w[:], k.XT[:, b * CW:(b + 1) * CW], start=True, stop=True
                              ).then_inc(made, 1)

        @block.scalar
        def _(act):
            for b in range(NCW):
                act.wait_ge(made, b + 1)
                act.activation(QT[:, b * CW:(b + 1) * CW], ps[:, b, 0:CW], ACT.Copy, scale=float(D) ** -0.5
                               ).then_inc(copied, 1)

        @block.vector
        def _(dve):
            for b in range(NCW):
                dve.wait_ge(made, NCW + b + 1)
                dve.tensor_copy(KT[:, b * CW:(b + 1) * CW], ps[:, b, 0:CW])


def attention_max(nc, k, QT, KT, shift):
    with ExitStack() as ctx:
        def sb(name, shape, dt=F32):
            return ctx.enter_context(nc.sbuf_tensor(name, shape, dt))

        def sem(name):
            return ctx.enter_context(nc.semaphore(name))

        ring = sb("am_ring", [P, UN, NP])
        left = sb("am_left", [P, UN, P])
        closed = sb("am_closed", [P, NP], BF16)
        unread = sb("am_unread", [P, 2, HB, CW], BF16)
        best_u = sb("am_best_u", [P, UN, 2])
        best = sb("am_best", [P, NT])
        best_t = sb("am_best_t", [NT, P])
        parts = sb("am_parts", [NT, 3, P], BF16)
        rest = sb("am_rest", [NT, P])
        whole = sb("am_whole", [NT, P])
        ps = ctx.enter_context(nc.psum_tensor("am_ps", [P, 8, BANK], F32))
        loaded = [sem(f"am_loaded{u}") for u in range(UN)]
        held = sem("am_held")
        left_ready, scored, taken, masked, chain, turned, parts_ready, stored, shift_in, best_ready = map(
            sem, ("am_left_ready", "am_scored", "am_taken", "am_masked", "am_chain", "am_turned", "am_parts_ready",
                  "am_stored", "am_shift_in", "am_best_ready"))
        block = ctx.enter_context(nc.Block())
        rows = k.count_rs.rearrange("(t p) c -> t p c", p=P)

        @block.sync
        def _(sp):
            with sp.Fori(0, NT // UN) as lap:
                for u in range(UN):
                    t = lap * UN + u
                    sp.wait_ge(masked, t + 1)
                    sp.dma_start(ring[:, u, :].unsqueeze(1), rows[bass.ds(t, 1)].rearrange("t p c -> p t c")
                                 ).then_inc(loaded[u], 16)
            sp.wait_ge(parts_ready, 1)
            sp.dma_start(k.shift_d.rearrange("s (t p) -> t s p", p=P), parts[:]).then_inc(stored, 16)
            sp.wait_ge(stored, 16)
            sp.dma_start(shift[:], k.shift_d).then_inc(shift_in, 16)
            sp.wait_ge(shift_in, 16)

        @block.gpsimd
        def _(pool):
            with pool.Fori(0, NT // UN) as lap:
                for u in range(UN):
                    t = lap * UN + u
                    pool.wait_ge(scored, t * 2 + 2)
                    pool.tensor_copy(left[:, u, :], QT[:, bass.ds(t * P, P)]).then_inc(left_ready, 1)

        @block.tensor
        def _(pe):
            pe.sem_inc(scored, 2 * UN)
            with pe.Fori(0, NT // UN) as lap:
                for u in range(UN):
                    t = lap * UN + u
                    pe.wait_ge(left_ready, t + 1)
                    for s in range(2):
                        pe.wait_ge(taken, t * 2 + (s + 1))
                        for b in range(s * HB, (s + 1) * HB):
                            last = pe.matmul(ps[:, b, 0:CW], left[:, u, :], KT[:, b * CW:(b + 1) * CW],
                                             start=True, stop=True)
                        last.then_inc(scored, 1)
            pe.wait_ge(best_ready, 1)
            pe.transpose(ps[0:NT, 0, 0:P], best[:], k.ident[:]).then_inc(turned, 1)

        @block.vector
        def _(dve):
            dve.sem_inc(masked, UN)
            dve.sem_inc(taken, 2)
            with dve.Fori(0, NT // UN) as lap:
                for u in range(UN):
                    t = lap * UN + u
                    dve.wait_ge(loaded[u], lap * 16 + 16)
                    dve.wait_ge(taken, t * 2 + 2)
                    dve.tensor_scalar(closed[:], ring[:, u, :], 0.0, -BIG, ALU.is_equal, ALU.mult
                                      ).then_inc(masked, 1)
                    dve.wait_ge(masked, t + (UN + 1))
                    for s in range(2):
                        hold(dve, scored, t * 2 + (2 * UN + s + 1), held)
                        dve.tensor_tensor_reduce(
                            out=unread[:, s], in0=closed[:, s * HALF:(s + 1) * HALF].rearrange("p (b c) -> p b c", c=CW),
                            in1=ps[:, s * HB:(s + 1) * HB, 0:CW], scale=1.0, scalar=-3.0e38, op0=ALU.add, op1=ALU.max,
                            accum_out=best_u[:, u, s:s + 1]).then_inc(taken, 1)
                dve.wait_ge(taken, lap * (2 * UN) + (2 * UN + 2))
                dve.tensor_tensor(best[:, bass.ds(lap * UN, UN)], best_u[:, :, 0], best_u[:, :, 1], ALU.max
                                  ).then_inc(chain, 1)
                dve.wait_ge(chain, lap + 1)
            dve.sem_inc(best_ready, 1)
            dve.wait_ge(turned, 1)
            ch = Chain(dve, chain)
            ch.n = NT // UN
            ch.step(dve.tensor_scalar(best_t[:], ps[0:NT, 0, 0:P], -1.0, None, ALU.mult))
            ch.step(dve.tensor_copy(parts[:, 0], best_t[:]))
            ch.step(dve.tensor_copy(whole[:], parts[:, 0]))
            ch.step(dve.tensor_tensor(rest[:], best_t[:], whole[:], ALU.subtract))
            ch.step(dve.tensor_copy(parts[:, 1], rest[:]))
            ch.step(dve.tensor_copy(whole[:], parts[:, 1]))
            ch.step(dve.tensor_tensor(rest[:], rest[:], whole[:], ALU.subtract))
            dve.tensor_copy(parts[:, 2], rest[:]).then_inc(parts_ready, 1)


def attend(nc, k, QT, KT, shift, acc_t, psum_p):
    with ExitStack() as ctx:
        def sb(name, shape, dt=F32):
            return ctx.enter_context(nc.sbuf_tensor(name, shape, dt))

        def sem(name):
            return ctx.enter_context(nc.semaphore(name))

        count = sb("at_count", [P, UN, HALF])
        p = sb("at_p", [P, UN, HALF])
        keys = sb("at_keys", [P, UN, P])
        states = sb("at_states", [P, UN, D])
        ones = sb("at_ones", [3, P], BF16)
        ps = ctx.enter_context(nc.psum_tensor("at_ps", [P, 8, BANK], F32))
        loaded = [sem(f"at_loaded{u}") for u in range(UN)]
        ones_set, left_ready, scored, bounded, exps, probs, used, added, copied = map(
            sem, ("at_ones_set", "at_left_ready", "at_scored", "at_bounded", "at_exps", "at_probs", "at_used", "at_added",
                  "at_copied"))
        block = ctx.enter_context(nc.Block())
        rows = k.count_sr.rearrange("(t p) (s c) -> t s p c", p=P, s=2)

        @block.sync
        def _(sp):
            for s in range(2):
                with sp.Fori(0, NT // UN) as lap:
                    for u in range(UN):
                        t = lap * UN + u
                        sp.wait_ge(probs, t + (s * NT + 1))
                        sp.dma_start(count[:, u, :].unsqueeze(1), rows[bass.ds(t, 1), s].rearrange("t p c -> p t c")
                                     ).then_inc(loaded[u], 16)

        @block.gpsimd
        def _(pool):
            pool.memset(ones[:], 1.0).then_inc(ones_set, 1)
            for s in range(2):
                with pool.Fori(0, NT // UN) as lap:
                    for u in range(UN):
                        t = lap * UN + u
                        pool.wait_ge(used, t + (s * NT + 1))
                        pool.tensor_copy(keys[:, u, :], KT[:, bass.ds(t * P, P)])
                        pool.tensor_copy(states[:, u, :].unsqueeze(1), k.X[:, bass.ds(t, 1), :]).then_inc(left_ready, 1)

        @block.tensor
        def _(pe):
            pe.sem_inc(used, UN)
            pe.wait_ge(ones_set, 1)
            for s in range(2):
                if s:
                    pe.wait_ge(copied, 1)
                for b in range(HB):
                    pe.matmul(ps[:, HB + b, 0:CW], k.zeros[:, 0:P], k.zeros[:, 0:CW], start=True, stop=True)
                with pe.Fori(0, NT // UN) as lap:
                    def score(u):
                        t = lap * UN + u
                        pe.wait_ge(left_ready, t + (s * NT + 1))
                        pe.wait_ge(bounded, t + (s * NT + 1))
                        for b in range(HB):
                            cols = slice(s * HALF + b * CW, s * HALF + (b + 1) * CW)
                            pe.matmul(ps[:, b, 0:CW], keys[:, u, :], QT[:, cols], start=True, stop=False)
                            last = pe.matmul(ps[:, b, 0:CW], ones[:], shift[:, cols], start=False, stop=True)
                        last.then_inc(scored, 1)

                    def gather(u):
                        pe.wait_ge(probs, lap * UN + (s * NT + u + UN + 1))
                        for b in range(HB):
                            last = pe.matmul(ps[:, HB + b, 0:CW], states[:, u, :], p[:, u, b * CW:(b + 1) * CW],
                                             start=False, stop=True, skip_group_check=True)
                        last.then_inc(used, 1)

                    score(0)
                    for u in range(1, UN):
                        score(u)
                        gather(u - 1)
                    gather(UN - 1)

        @block.scalar
        def _(act):
            act.sem_inc(bounded, 1)
            for s in range(2):
                with act.Fori(0, NT // UN) as lap:
                    for u in range(UN):
                        t = lap * UN + u
                        act.wait_ge(scored, t + (s * NT + 1))
                        act.wait_ge(used, t + (s * NT + 1))
                        act.wait_ge(added, t + (s * NT + 1))
                        act.activation(p[:, u, :].rearrange("p (b c) -> p b c", c=CW), ps[:, 0:HB, 0:CW], ACT.Relu,
                                       scale=-1.0).then_inc(bounded, 1)
                        act.wait_ge(bounded, t + (s * NT + 2))
                        act.activation(p[:, u, :], p[:, u, :], ACT.Exp, scale=-1.0).then_inc(exps, 1)
                act.wait_ge(used, UN + (s + 1) * NT)
                act.activation(acc_t[:, s * HALF:(s + 1) * HALF].rearrange("p (b c) -> p b c", c=CW),
                               ps[:, HB:NCW, 0:CW], ACT.Copy).then_inc(copied, 1)

        @block.vector
        def _(dve):
            dve.sem_inc(probs, UN)
            dve.memset(psum_p, 0.0).then_inc(added, UN)
            for s in range(2):
                with dve.Fori(0, NT // UN) as lap:
                    for u in range(UN):
                        t = lap * UN + u
                        dve.wait_ge(exps, t + (s * NT + 1))
                        dve.wait_ge(loaded[u], lap * 16 + (s * 16 * (NT // UN) + 16))
                        dve.tensor_tensor(p[:, u, :], p[:, u, :], count[:, u, :], ALU.mult).then_inc(probs, 1)
                        dve.wait_ge(probs, t + (s * NT + UN + 1))
                        dve.wait_ge(added, t + (s * NT + UN))
                        dve.tensor_tensor(psum_p[:, s * HALF:(s + 1) * HALF], psum_p[:, s * HALF:(s + 1) * HALF],
                                          p[:, u, :], ALU.add).then_inc(added, 1)


def finish_attention(nc, k, acc_t, psum_p):
    with ExitStack() as ctx:
        def sb(name, shape, dt=F32):
            return ctx.enter_context(nc.sbuf_tensor(name, shape, dt))

        def sem(name):
            return ctx.enter_context(nc.semaphore(name))

        wv = sb("fa_wv", [D, D])
        wo = sb("fa_wo", [D, D])
        ones = sb("fa_ones", [P, 1])
        values_t = sb("fa_values", [P, NP])
        inv = sb("fa_inv", [P, NT])
        T = sb("fa_t", [P, NT, D])
        b = NormBuffers(sb, "att")
        ps = ctx.enter_context(nc.psum_tensor("fa_ps", [P, 8, BANK], F32))
        loaded, ones_set, valued, copied, projected, chain, var_ready, root_ready, x_ready, x_turned = map(
            sem, ("fa_loaded", "fa_ones_set", "fa_valued", "fa_copied", "fa_projected", "fa_chain", "fa_var",
                  "fa_root", "fa_x", "fa_turned"))
        block = ctx.enter_context(nc.Block())

        @block.sync
        def _(sp):
            sp.dma_start(wv[:], k.L2_gnn_Wv).then_inc(loaded, 16)
            sp.dma_start(wo[:], k.L2_gnn_Wo).then_inc(loaded, 16)

        @block.gpsimd
        def _(pool):
            pool.memset(ones[:], 1.0).then_inc(ones_set, 1)

        @block.tensor
        def _(pe):
            pe.wait_ge(loaded, 32)
            for bank in range(NCW):
                last = pe.matmul(ps[:, bank, 0:CW], wv[:], acc_t[:, bank * CW:(bank + 1) * CW], start=True, stop=True)
            last.then_inc(valued, 1)
            pe.wait_ge(copied, 1)
            project(pe, ps, [values_t], [wo[:]])
            pe.wait_ge(ones_set, 1)
            for t in range(NT):
                last = pe.matmul(ps[:, 7, t:t + 1], psum_p[:, t * P:(t + 1) * P], ones[:], start=True, stop=True,
                                 skip_group_check=True)
            last.then_inc(projected, 1)
            pe.wait_ge(x_ready, 1)
            turn(pe, ps, k.X, k.ident[:]).then_inc(x_turned, 1)

        @block.scalar
        def _(act):
            act.wait_ge(valued, 1)
            act.activation(values_t[:].rearrange("p (b c) -> p b c", c=CW), ps[:, :, 0:CW], ACT.Copy
                           ).then_inc(copied, 1)
            root(act, b, var_ready, root_ready, 1)
            act.wait_ge(x_turned, 1)
            act.activation(k.XT[:], flat(ps), ACT.Copy)

        @block.vector
        def _(dve):
            ch = Chain(dve, chain)
            dve.wait_ge(projected, 1)
            ch.step(dve.tensor_scalar(inv[:], ps[:, 7, 0:NT], 1e-30, None, ALU.max))
            ch.step(dve.reciprocal(inv[:], inv[:]))
            ch.step(dve.tensor_tensor(T[:], tiles_of(ps), inv[:].unsqueeze(2).to_broadcast([P, NT, D]), ALU.mult))
            ch.step(dve.tensor_tensor(T[:], T[:], k.X[:], ALU.add))
            ch.step(dve.tensor_tensor(T[:], T[:], k.X[:], ALU.add))
            normalise(dve, ch, b, T[:], k.X[:], var_ready, root_ready, 1)
            dve.sem_inc(x_ready, 1)


def degrees(nc, k, inv_deg):
    with ExitStack() as ctx:
        ring = ctx.enter_context(nc.sbuf_tensor("dg_ring", [P, UN, NP], F32))
        total = ctx.enter_context(nc.sbuf_tensor("dg_total", [P, NP], F32))
        ones = ctx.enter_context(nc.sbuf_tensor("dg_ones", [P, P], F32))
        ps = ctx.enter_context(nc.psum_tensor("dg_ps", [P, 8, BANK], F32))
        loaded = [ctx.enter_context(nc.semaphore(f"dg_loaded{u}")) for u in range(UN)]
        added = ctx.enter_context(nc.semaphore("dg_added"))
        ones_set = ctx.enter_context(nc.semaphore("dg_ones_set"))
        summed = ctx.enter_context(nc.semaphore("dg_summed"))
        chain = ctx.enter_context(nc.semaphore("dg_chain"))
        block = ctx.enter_context(nc.Block())
        rows = k.count_sr.rearrange("(t p) c -> t p c", p=P)

        @block.sync
        def _(sp):
            with sp.Fori(0, NT // UN) as lap:
                for u in range(UN):
                    t = lap * UN + u
                    sp.wait_ge(added, t + 1)
                    sp.dma_start(ring[:, u, :].unsqueeze(1), rows[bass.ds(t, 1)].rearrange("t p c -> p t c")
                                 ).then_inc(loaded[u], 16)

        @block.gpsimd
        def _(pool):
            pool.memset(ones[:], 1.0).then_inc(ones_set, 1)

        @block.tensor
        def _(pe):
            pe.wait_ge(ones_set, 1)
            pe.wait_ge(added, UN + NT)
            for b in range(NCW):
                last = pe.matmul(ps[:, b, 0:CW], ones[:], total[:, b * CW:(b + 1) * CW], start=True, stop=True)
            last.then_inc(summed, 1)

        @block.vector
        def _(dve):
            dve.memset(total[:], 0.0).then_inc(added, UN)
            with dve.Fori(0, NT // UN) as lap:
                for u in range(UN):
                    dve.wait_ge(loaded[u], lap * 16 + 16)
                    dve.wait_ge(added, lap * UN + (UN + u))
                    dve.tensor_tensor(total[:], total[:], ring[:, u, :], ALU.add).then_inc(added, 1)
            ch = Chain(dve, chain)
            dve.wait_ge(summed, 1)
            ch.step(dve.tensor_scalar(inv_deg[:].rearrange("p (b c) -> p b c", c=CW), ps[:, :, 0:CW], 1.0, None,
                                      ALU.max))
            ch.step(dve.reciprocal(inv_deg[:], inv_deg[:]))


def sage_hidden(nc, k, agg, inv_deg, Y, own_t):
    with ExitStack() as ctx:
        def sb(name, shape, dt=F32):
            return ctx.enter_context(nc.sbuf_tensor(name, shape, dt))

        def sem(name):
            return ctx.enter_context(nc.semaphore(name))

        w1l = sb("sh_w1l", [D, 2 * D])
        w1r = sb("sh_w1r", [D, 2 * D])
        w2l = sb("sh_w2l", [D, 2, D])
        w2r = sb("sh_w2r", [D, 2, D])
        b1 = sb("sh_b1", [D, 2])
        b2 = sb("sh_b2", [D, 1])
        hidden = sb("sh_hidden", [D, 2, NP])
        ps = ctx.enter_context(nc.psum_tensor("sh_ps", [P, 8, BANK], F32))
        loaded, scaled, made, hid, y_made, y_out, own_made = map(
            sem, ("sh_loaded", "sh_scaled", "sh_made", "sh_hid", "sh_y_made", "sh_y_out", "sh_own_made"))
        block = ctx.enter_context(nc.Block())

        @block.sync
        def _(sp):
            sp.dma_start(w1l[:], k.L3_gnn_w1_l).then_inc(loaded, 16)
            sp.dma_start(w1r[:], k.L3_gnn_w1_r).then_inc(loaded, 16)
            sp.dma_start(w2l[:], k.L3_gnn_w2_l.rearrange("(h p) d -> p h d", p=P)).then_inc(loaded, 16)
            sp.dma_start(w2r[:], k.L3_gnn_w2_r.rearrange("(h p) d -> p h d", p=P)).then_inc(loaded, 16)
            for h in range(2):
                sp.dma_start(b1[:, h:h + 1], k.L3_gnn_b1[h * D:(h + 1) * D].rearrange("(p a) -> p a", a=1)
                             ).then_inc(loaded, 16)
            sp.dma_start(b2[:], k.L3_gnn_b2.rearrange("(p a) -> p a", a=1)).then_inc(loaded, 16)

        @block.tensor
        def _(pe):
            pe.wait_ge(loaded, 7 * 16)
            pe.wait_ge(scaled, 1)
            for h in range(2):
                for b in range(NCW):
                    if h:
                        pe.wait_ge(hid, b + 1)
                    pe.matmul(ps[:, b, 0:CW], w1l[:, h * D:(h + 1) * D], agg[:, b * CW:(b + 1) * CW],
                              start=True, stop=False)
                    pe.matmul(ps[:, b, 0:CW], w1r[:, h * D:(h + 1) * D], k.XT[:, b * CW:(b + 1) * CW],
                              start=False, stop=True).then_inc(made, 1)
            pe.wait_ge(hid, 2 * NCW)
            project(pe, ps, [hidden[:, 0], hidden[:, 1]], [w2l[:, 0], w2l[:, 1]]).then_inc(y_made, 1)
            pe.wait_ge(y_out, 1)
            for b in range(NCW):
                for h in range(2):
                    last = pe.matmul(ps[:, b, 0:CW], w2r[:, h], hidden[:, h, b * CW:(b + 1) * CW],
                                     start=h == 0, stop=h == 1)
            last.then_inc(own_made, 1)

        @block.vector
        def _(dve):
            dve.tensor_tensor(agg[:], agg[:], inv_deg[:], ALU.mult).then_inc(scaled, 1)
            dve.wait_ge(y_made, 1)
            dve.tensor_copy(Y[:], tiles_of(ps)).then_inc(y_out, 1)

        @block.scalar
        def _(act):
            for h in range(2):
                for b in range(NCW):
                    act.wait_ge(made, h * NCW + b + 1)
                    act.activation(hidden[:, h, b * CW:(b + 1) * CW], ps[:, b, 0:CW], ACT.Relu, bias=b1[:, h:h + 1]
                                   ).then_inc(hid, 1)
            act.wait_ge(own_made, 1)
            act.activation(own_t[:].rearrange("p (b c) -> p b c", c=CW), ps[:, :, 0:CW], ACT.Identity, bias=b2[:])


def finish_sage(nc, k, agg, inv_deg, own_t):
    with ExitStack() as ctx:
        def sb(name, shape, dt=F32):
            return ctx.enter_context(nc.sbuf_tensor(name, shape, dt))

        def sem(name):
            return ctx.enter_context(nc.semaphore(name))

        T = sb("fs_t", [P, NT, D])
        b = NormBuffers(sb, "sage")
        ps = ctx.enter_context(nc.psum_tensor("fs_ps", [P, 8, BANK], F32))
        chain, z_ready, gated, turned, var_ready, root_ready, x_ready, stored = map(
            sem, ("fs_chain", "fs_z", "fs_gated", "fs_turned", "fs_var", "fs_root", "fs_x", "fs_stored"))
        block = ctx.enter_context(nc.Block())

        @block.vector
        def _(dve):
            ch = Chain(dve, chain)
            ch.step(dve.tensor_tensor(agg[:], agg[:], inv_deg[:], ALU.mult))
            dve.tensor_tensor(agg[:], agg[:], own_t[:], ALU.add).then_inc(z_ready, 1)
            dve.wait_ge(turned, 1)
            ch.step(dve.tensor_tensor(T[:], tiles_of(ps), k.X[:], ALU.add))
            normalise(dve, ch, b, T[:], T[:], var_ready, root_ready, 1)
            dve.sem_inc(x_ready, 1)

        @block.scalar
        def _(act):
            act.wait_ge(z_ready, 1)
            act.activation(agg[:], agg[:], ACT.Sigmoid).then_inc(gated, 1)
            root(act, b, var_ready, root_ready, 1)

        @block.tensor
        def _(pe):
            pe.wait_ge(gated, 1)
            turn_back(pe, ps, agg, k.ident[:]).then_inc(turned, 1)

        @block.sync
        def _(sp):
            sp.wait_ge(x_ready, 1)
            sp.dma_start(k.out[0:(NT - 1) * P, :].rearrange("(t p) d -> p t d", p=P), T[:, 0:NT - 1, :]
                         ).then_inc(stored, 16)
            sp.dma_start(k.out[(NT - 1) * P:N, :], T[0:REST, NT - 1, :]).then_inc(stored, 16)
            sp.wait_ge(stored, 32)


def clear_semaphores(nc):
    free = nc.free_semaphores
    assert len(free) == max(free) - min(free) + 1
    with nc.Block() as block:
        @block.gpsimd
        def _(pool):
            pool.sem_clear(range(min(free), max(free) + 1))


def dump(nc, k, name, tensor):
    with nc.semaphore(f"{name}_dumped") as done, nc.Block() as block:
        target = k.dram(name, tuple(tensor.shape))

        @block.sync
        def _(sp):
            sp.dma_start(target, tensor[:]).then_inc(done, 16)
            sp.wait_ge(done, 16)


def program(nc, ins, out, stop=99, debug=None):
    k = Kernel(ins, out)
    kind = "ExternalOutput" if debug is not None else "Internal"

    def dram(name, shape, dt=F32):
        return nc.dram_tensor(name, shape, dt, kind=kind).ap()

    k.table_d = dram("window_table", (NW, 3), I32)
    adj = dram("adjacency", (2, NP * NP))
    k.adj_w = adj.rearrange("v (w p c) -> w p v c", w=NW, p=P)
    k.count_rs = adj[0].rearrange("(r s) -> r s", s=NP)
    k.weight_rs = adj[1].rearrange("(r s) -> r s", s=NP)
    k.count_sr = dram("count_by_source", (NP, NP))
    rows_d = dram("gat_rows_d", (2 * HEADS, NP))
    u_d = dram("gat_u_d", (2 * HEADS, NP))
    sums_d = dram("gat_sums_d", (HEADS, C + 1, NP))
    k.shift_d = dram("shift_d", (3, NP), BF16)
    k.dram = dram

    with ExitStack() as ctx:
        def sb(name, shape, dt=F32):
            return ctx.enter_context(nc.sbuf_tensor(name, shape, dt))

        k.X = sb("X", [P, NT, D])
        k.ident = sb("ident", [P, P])
        k.zeros = sb("zeros", [P, CW], BF16)
        with ExitStack() as edges:
            def esb(name, shape, dt=F32):
                return edges.enter_context(nc.sbuf_tensor(name, shape, dt))

            k.table = esb("table", [1, NW * 3], I32)
            k.cols = esb("cols", [P, 5, ECOL])
            k.iota_low = esb("iota_low", [P, SL], I16)
            k.iota_key = esb("iota_key", [P, P], I16)
            k.key_base = esb("key_base", [P, NW])
            edge_tables(nc, k)
            if stop >= 1:
                build_matrices(nc, k)
        k.XT = sb("XT", [P, NP])
        if stop >= 2:
            with nc.sbuf_tensor("agg0", [P, NP], F32) as agg:
                aggregate(nc, k, "agg_gcn", k.weight_rs, k.X, agg)
                finish_gcn(nc, k, agg)
            if debug is not None:
                dump(nc, k, "x1", k.X)
        if stop >= 3:
            with (nc.sbuf_tensor("heads", [P, HEADS, NT, C + 1], F32) as heads,
                  nc.sbuf_tensor("att_cols", [P, 2 * HEADS, NT], F32) as cols,
                  nc.sbuf_tensor("best", [P, HEADS, NT], F32) as best,
                  nc.sbuf_tensor("own_p", [P, HEADS, NT], F32) as own):
                gat_project(nc, k, heads, cols, rows_d)
                gat_max(nc, k, rows_d, best)
                gat_exponents(nc, k, cols, best, own, u_d)
                gat_attend(nc, k, heads, cols, u_d, sums_d)
                finish_gat(nc, k, sums_d, heads, own)
            if debug is not None:
                dump(nc, k, "x2", k.X)
        if stop >= 4:
            clear_semaphores(nc)
            with (nc.sbuf_tensor("QT", [P, NP], F32) as QT, nc.sbuf_tensor("KT", [P, NP], F32) as KT,
                  nc.sbuf_tensor("shift", [3, NP], BF16) as shift):
                attention_project(nc, k, QT, KT)
                attention_max(nc, k, QT, KT, shift)
                with (nc.sbuf_tensor("acc_t", [P, NP], F32) as acc_t,
                      nc.sbuf_tensor("psum_p", [P, NP], F32) as psum_p):
                    attend(nc, k, QT, KT, shift, acc_t, psum_p[:])
                    finish_attention(nc, k, acc_t, psum_p)
            if debug is not None:
                dump(nc, k, "x3", k.X)
        if stop >= 5:
            clear_semaphores(nc)
            with (nc.sbuf_tensor("inv_deg", [P, NP], F32) as inv_deg, nc.sbuf_tensor("Y", [P, NT, D], F32) as Y,
                  nc.sbuf_tensor("own_t", [P, NP], F32) as own_t, nc.sbuf_tensor("agg3", [P, NP], F32) as agg):
                degrees(nc, k, inv_deg)
                aggregate(nc, k, "sage1", k.count_sr, k.X, agg)
                sage_hidden(nc, k, agg, inv_deg, Y, own_t)
                aggregate(nc, k, "sage2", k.count_sr, Y, agg)
                finish_sage(nc, k, agg, inv_deg, own_t)


_INS = ["x", "src", "dst", "edge_weight", "L0_gnn_weight", "L0_gnn_b", "L1_gnn_W", "L1_gnn_att_src",
        "L1_gnn_att_dst", "L1_gnn_gat_bias", "L1_gnn_skip_W", "L1_gnn_skip_b", "L1_gnn_ln_g", "L1_gnn_ln_b",
        "L2_gnn_Wq", "L2_gnn_Wk", "L2_gnn_Wv", "L2_gnn_Wo", "L3_gnn_w1_l", "L3_gnn_w1_r", "L3_gnn_b1",
        "L3_gnn_w2_l", "L3_gnn_w2_r", "L3_gnn_b2"]


def kernel(**inputs):
    import numpy as _np
    import concourse.bacc as _bacc
    from concourse import mybir as _mybir
    from concourse.bass_utils import run_bass_kernel_spmd as _run

    nc = _bacc.Bacc("TRN2", target_bir_lowering=False, num_devices=1)
    arrays, ins = {}, {}
    for name in _INS:
        a = _np.ascontiguousarray(inputs[name])
        arrays[f"in_{name}_dram"] = a
        ins[name] = nc.dram_tensor(f"in_{name}_dram", a.shape, _mybir.dt.from_np(a.dtype), kind="ExternalInput").ap()
    out = nc.dram_tensor("out_0_dram", (N, D), _mybir.dt.float32, kind="ExternalOutput").ap()
    program(nc, ins, out)
    r = _run(nc, [arrays], core_ids=[0])
    return r.results[0]["out_0_dram"]
```
